# Optimizing a Trainium2 kernel written in Bass

```python
import numpy as np
import jax
import jax.numpy as jnp

def _softmax(x, axis=-1):
    return jax.nn.softmax(x, axis=axis)

def _gelu(x):
    return jax.nn.gelu(x, approximate=True)

def _silu(x):
    return jax.nn.silu(x)

def _sigmoid(x):
    return jax.nn.sigmoid(x)

def _layernorm(x, axis=-1, eps=1e-05):
    m = jnp.mean(x, axis=axis, keepdims=True)
    v = jnp.var(x, axis=axis, keepdims=True)
    return (x - m) / jnp.sqrt(v + eps)

def _scatter_add(tgt, idx, src, axis=0):
    return tgt.at[idx].add(src)

def _segment_sum(src, seg, n):
    return jax.ops.segment_sum(src, seg, n)
kernel_name = 'mk_dlrm_tower_d1_rec_r8_a03df4'

def setup_inputs(seed: int=0):
    np.random.seed(seed)
    _w = jnp.asarray

    def _rec_inputs():
        import jax
        import jax.numpy as jnp
        _tk = jax.random.key(seed)
        ids = jnp.stack([jax.random.randint(jax.random.fold_in(_tk, 200 + f), (512,), 0, v, jnp.int32) for f, v in enumerate([125000, 1000, 12500, 12500, 1250, 12500, 1250, 1000, 1000, 1000, 1000, 1000, 12500, 1000, 1000, 1000, 1250, 12500, 1000, 1250, 1250, 1250, 12500, 12500, 12500, 1000])], axis=1)
        tbl_0 = 0.05 * jax.random.normal(jax.random.fold_in(_tk, 500 + 0), (125000, 128), jnp.float32)
        tbl_1 = 0.05 * jax.random.normal(jax.random.fold_in(_tk, 500 + 1), (1000, 128), jnp.float32)
        tbl_2 = 0.05 * jax.random.normal(jax.random.fold_in(_tk, 500 + 2), (12500, 128), jnp.float32)
        tbl_3 = 0.05 * jax.random.normal(jax.random.fold_in(_tk, 500 + 3), (12500, 128), jnp.float32)
        tbl_4 = 0.05 * jax.random.normal(jax.random.fold_in(_tk, 500 + 4), (1250, 128), jnp.float32)
        tbl_5 = 0.05 * jax.random.normal(jax.random.fold_in(_tk, 500 + 5), (12500, 128), jnp.float32)
        tbl_6 = 0.05 * jax.random.normal(jax.random.fold_in(_tk, 500 + 6), (1250, 128), jnp.float32)
        tbl_7 = 0.05 * jax.random.normal(jax.random.fold_in(_tk, 500 + 7), (1000, 128), jnp.float32)
        tbl_8 = 0.05 * jax.random.normal(jax.random.fold_in(_tk, 500 + 8), (1000, 128), jnp.float32)
        tbl_9 = 0.05 * jax.random.normal(jax.random.fold_in(_tk, 500 + 9), (1000, 128), jnp.float32)
        tbl_10 = 0.05 * jax.random.normal(jax.random.fold_in(_tk, 500 + 10), (1000, 128), jnp.float32)
        tbl_11 = 0.05 * jax.random.normal(jax.random.fold_in(_tk, 500 + 11), (1000, 128), jnp.float32)
        tbl_12 = 0.05 * jax.random.normal(jax.random.fold_in(_tk, 500 + 12), (12500, 128), jnp.float32)
        tbl_13 = 0.05 * jax.random.normal(jax.random.fold_in(_tk, 500 + 13), (1000, 128), jnp.float32)
        tbl_14 = 0.05 * jax.random.normal(jax.random.fold_in(_tk, 500 + 14), (1000, 128), jnp.float32)
        tbl_15 = 0.05 * jax.random.normal(jax.random.fold_in(_tk, 500 + 15), (1000, 128), jnp.float32)
        tbl_16 = 0.05 * jax.random.normal(jax.random.fold_in(_tk, 500 + 16), (1250, 128), jnp.float32)
        tbl_17 = 0.05 * jax.random.normal(jax.random.fold_in(_tk, 500 + 17), (12500, 128), jnp.float32)
        tbl_18 = 0.05 * jax.random.normal(jax.random.fold_in(_tk, 500 + 18), (1000, 128), jnp.float32)
        tbl_19 = 0.05 * jax.random.normal(jax.random.fold_in(_tk, 500 + 19), (1250, 128), jnp.float32)
        tbl_20 = 0.05 * jax.random.normal(jax.random.fold_in(_tk, 500 + 20), (1250, 128), jnp.float32)
        tbl_21 = 0.05 * jax.random.normal(jax.random.fold_in(_tk, 500 + 21), (1250, 128), jnp.float32)
        tbl_22 = 0.05 * jax.random.normal(jax.random.fold_in(_tk, 500 + 22), (12500, 128), jnp.float32)
        tbl_23 = 0.05 * jax.random.normal(jax.random.fold_in(_tk, 500 + 23), (12500, 128), jnp.float32)
        tbl_24 = 0.05 * jax.random.normal(jax.random.fold_in(_tk, 500 + 24), (12500, 128), jnp.float32)
        tbl_25 = 0.05 * jax.random.normal(jax.random.fold_in(_tk, 500 + 25), (1000, 128), jnp.float32)
        _rk = jax.random.fold_in(_tk, 7)
        r_dense_features = -0.000520686 + 1.00062 * jax.random.normal(jax.random.fold_in(_rk, 101), (512, 128), jnp.float32)
        W_top1 = 0.0405887 * jax.random.normal(jax.random.fold_in(_tk, 801), (607, 512), jnp.float32)
        W_top2 = 0.0441942 * jax.random.normal(jax.random.fold_in(_tk, 802), (512, 256), jnp.float32)
        W_top3 = 0.0625 * jax.random.normal(jax.random.fold_in(_tk, 803), (256, 1), jnp.float32)
        b_top1 = jnp.zeros((512,), jnp.float32)
        b_top2 = jnp.zeros((256,), jnp.float32)
        return (r_dense_features, ids, tbl_0, tbl_1, tbl_2, tbl_3, tbl_4, tbl_5, tbl_6, tbl_7, tbl_8, tbl_9, tbl_10, tbl_11, tbl_12, tbl_13, tbl_14, tbl_15, tbl_16, tbl_17, tbl_18, tbl_19, tbl_20, tbl_21, tbl_22, tbl_23, tbl_24, tbl_25, W_top1, b_top1, W_top2, b_top2, W_top3)
    r_dense_features, ids, tbl_0, tbl_1, tbl_2, tbl_3, tbl_4, tbl_5, tbl_6, tbl_7, tbl_8, tbl_9, tbl_10, tbl_11, tbl_12, tbl_13, tbl_14, tbl_15, tbl_16, tbl_17, tbl_18, tbl_19, tbl_20, tbl_21, tbl_22, tbl_23, tbl_24, tbl_25, W_top1, b_top1, W_top2, b_top2, W_top3 = _rec_inputs()

    def _L0_rec_setup():
        import jax, jax.numpy as jnp
        import numpy as np
        F = 26
        N = F + 1
        _TRIU_I, _TRIU_J = np.triu_indices(N, k=1)
        key = jax.random.key(seed)
        k1, k2 = jax.random.split(key)
        B, D = (2048, 128)
        dense_features = jax.random.normal(k1, (B, D), dtype=jnp.float32)
        sparse_features = jax.random.normal(k2, (B, F, D), dtype=jnp.float32)
        return {'dense_features': dense_features, 'sparse_features': sparse_features}
    _L0_rec_all = _L0_rec_setup()
    _L0_rec_in = {k: v for k, v in _L0_rec_all.items() if k in ()}
    del _L0_rec_all
    return {'r_dense_features': r_dense_features, 'ids': ids, 'tbl_0': tbl_0, 'tbl_1': tbl_1, 'tbl_2': tbl_2, 'tbl_3': tbl_3, 'tbl_4': tbl_4, 'tbl_5': tbl_5, 'tbl_6': tbl_6, 'tbl_7': tbl_7, 'tbl_8': tbl_8, 'tbl_9': tbl_9, 'tbl_10': tbl_10, 'tbl_11': tbl_11, 'tbl_12': tbl_12, 'tbl_13': tbl_13, 'tbl_14': tbl_14, 'tbl_15': tbl_15, 'tbl_16': tbl_16, 'tbl_17': tbl_17, 'tbl_18': tbl_18, 'tbl_19': tbl_19, 'tbl_20': tbl_20, 'tbl_21': tbl_21, 'tbl_22': tbl_22, 'tbl_23': tbl_23, 'tbl_24': tbl_24, 'tbl_25': tbl_25, 'W_top1': W_top1, 'b_top1': b_top1, 'W_top2': W_top2, 'b_top2': b_top2, 'W_top3': W_top3}

def reference(r_dense_features, ids, tbl_0, tbl_1, tbl_2, tbl_3, tbl_4, tbl_5, tbl_6, tbl_7, tbl_8, tbl_9, tbl_10, tbl_11, tbl_12, tbl_13, tbl_14, tbl_15, tbl_16, tbl_17, tbl_18, tbl_19, tbl_20, tbl_21, tbl_22, tbl_23, tbl_24, tbl_25, W_top1, b_top1, W_top2, b_top2, W_top3):
    import jax
    import jax.numpy as jnp

    def _L0_rec_ref(dense_features, sparse_features):
        import jax, jax.numpy as jnp
        import numpy as np
        F = 26
        N = F + 1
        _TRIU_I, _TRIU_J = np.triu_indices(N, k=1)
        combined = jnp.concatenate([dense_features[:, None, :], sparse_features], axis=1)
        interactions = jnp.einsum('bnd,bmd->bnm', combined, combined)
        interactions_flat = interactions[:, _TRIU_I, _TRIU_J]
        return jnp.concatenate([dense_features, interactions_flat], axis=1)
    e = jnp.stack([tbl_0[ids[:, 0]], tbl_1[ids[:, 1]], tbl_2[ids[:, 2]], tbl_3[ids[:, 3]], tbl_4[ids[:, 4]], tbl_5[ids[:, 5]], tbl_6[ids[:, 6]], tbl_7[ids[:, 7]], tbl_8[ids[:, 8]], tbl_9[ids[:, 9]], tbl_10[ids[:, 10]], tbl_11[ids[:, 11]], tbl_12[ids[:, 12]], tbl_13[ids[:, 13]], tbl_14[ids[:, 14]], tbl_15[ids[:, 15]], tbl_16[ids[:, 16]], tbl_17[ids[:, 17]], tbl_18[ids[:, 18]], tbl_19[ids[:, 19]], tbl_20[ids[:, 20]], tbl_21[ids[:, 21]], tbl_22[ids[:, 22]], tbl_23[ids[:, 23]], tbl_24[ids[:, 24]], tbl_25[ids[:, 25]]], axis=1)
    z = _L0_rec_ref(r_dense_features, e)
    z = z.reshape(z.shape[0], -1)
    h = jnp.concatenate([z, r_dense_features], axis=1)
    h = jnp.maximum(h @ W_top1 + b_top1, 0.0)
    h = jnp.maximum(h @ W_top2 + b_top2, 0.0)
    y = h @ W_top3
    return y

_drawn_inputs = setup_inputs


def setup_inputs(seed=0):
    import zlib

    import numpy as np

    out = dict(_drawn_inputs(seed))
    spreads = {'b_top1': (0.0, 0.1), 'b_top2': (0.0, 0.1)}
    factors = {}
    for name, (base, spread) in spreads.items():
        noise = np.random.default_rng([zlib.crc32(name.encode()), seed]).standard_normal(out[name].shape)
        drawn = base * np.exp(spread * noise) if base else spread * noise
        out[name] = jnp.asarray(drawn.astype(out[name].dtype))
    for name, factor in factors.items():
        out[name] = (out[name] * factor).astype(out[name].dtype)
    return out
```

```python
from contextlib import ExitStack

import concourse.bass as bass
from concourse import mybir

ALU = mybir.AluOpType
ACT = mybir.ActivationFunctionType
F32 = mybir.dt.float32
F32R = mybir.dt.float32r
I32 = mybir.dt.int32

P = 128
TABLES = 26
FEATURES = TABLES + 1
H1, H2 = 512, 256
M1, M2 = H1 // P, H2 // P

ONEHOT = [1, 7, 8, 9, 10, 11, 13, 14]
GATHERED = [f for f in range(TABLES) if f not in ONEHOT]
SLOTS = [0] + [f + 1 for f in GATHERED] + [f + 1 for f in ONEHOT]
PAD = 32

PER_GROUP = 4
IN_ROWS = 1 + len(GATHERED)
GROUPS = -(-IN_ROWS // PER_GROUP)
RING = 6

TBL_P = 125
OH_RING = 6
IDS_RING = 4

PAIR_COLS = FEATURES - 1
CHUNKS = -(-PAIR_COLS // 4)
BLOCK = 4
HALF_BLOCKS = 16


def pair_row(a, b):
    i, j = min(a, b), max(a, b)
    return P + i * FEATURES - i * (i + 1) // 2 + j - i - 1


def pe_order(tiles):
    order = []
    loaded = 0

    def group(n=1):
        nonlocal loaded
        for _ in range(n):
            if loaded < tiles * GROUPS:
                order.append(("group", loaded // GROUPS, loaded % GROUPS))
                loaded += 1

    for h in range(len(ONEHOT)):
        group()
        order.append(("onehot", h, 0))
    while loaded < GROUPS:
        group()
    for t in range(tiles):
        while loaded < (t + 1) * GROUPS:
            group()
        order.append(("gram", t, 0))
        if t:
            order.append(("l1", t - 1, 0))
        group(1)
        order.append(("gram", t, 1))
        if t:
            order += [("l2", t - 1, 0), ("l3", t - 1, 0)]
        group(1)
    order += [("l1", tiles - 1, 0), ("l2", tiles - 1, 0), ("l3", tiles - 1, 0)]
    return order


def dlrm_tower_kernel(nc, dense, ids, ids_rows, tables, w_pairs, w_dense, w_top2, columns, out):
    B = dense.shape[0]
    TILES = B // P
    NH = len(ONEHOT)
    depth = [tables[f].shape[0] // TBL_P for f in ONEHOT]
    DEPTH = max(depth)

    order = pe_order(TILES)
    units = [s for s in order if s[0] in ("group", "onehot")]
    unit_of = {s: n for n, s in enumerate(units)}
    last_unit = [max(unit_of["group", t, GROUPS - 1], max([unit_of["onehot", h, 0] for h in range(NH)], default=0)) for t in range(TILES)]

    def group_slots(g):
        return range(g * PER_GROUP, min((g + 1) * PER_GROUP, IN_ROWS))

    ctx = ExitStack()
    with ctx:
        def sb(name, shape, dt=F32):
            return ctx.enter_context(nc.sbuf_tensor(name, shape, dt))

        def pb(name, shape, dt=F32):
            return ctx.enter_context(nc.psum_tensor(name, shape, dt))

        def sem(name):
            return ctx.enter_context(nc.semaphore(name))

        feat_hi = sb("feat_hi", [P, B, PAD], F32R)
        feat_lo = sb("feat_lo", [P, B, PAD], F32R)
        dense_rows = sb("dense_rows", [P, TILES, P])
        dense_t = sb("dense_t", [P, B])
        rows = sb("rows", [P, RING, PER_GROUP, P])
        ids_sb = sb("ids_sb", [P, TILES, TABLES], I32)
        ident = sb("ident", [P, P])

        ids_all = sb("ids_all", [P, IDS_RING, B], I32)
        row_no_i = sb("row_no_i", [P, 2, DEPTH], I32)
        row_no = sb("row_no", [P, 2, DEPTH])
        tbl = sb("tbl", [P, 2, DEPTH, P])
        tbl_hi = sb("tbl_hi", [P, 2, DEPTH, P], F32R)
        tbl_lo = sb("tbl_lo", [P, 2, DEPTH, P], F32R)
        onehot = sb("onehot", [P, OH_RING, B], F32R)

        w1 = sb("w1", [P, CHUNKS, H1])
        late = ids_all[:, :, :].bitcast(F32)
        wd2 = late[:, 0:2, :]
        wd = wd2[:, 0, :]
        w2 = late[:, 2:4, :].rearrange("p a (b n) -> p (a b) n", n=H2)
        columns_sb = sb("columns_sb", [P, M2 + M1 + M2])
        w3, b1, b2 = columns_sb[:, 0:M2], columns_sb[:, M2:M2 + M1], columns_sb[:, M2 + M1:]
        pairs = tbl[:, :, :, :].rearrange("p a k d -> p (a k d)")[:, 0:2 * CHUNKS * P]\
            .rearrange("p (a c b) -> p a c b", a=2, c=CHUNKS)
        h1 = sb("h1", [P, M1, P])
        h2 = sb("h2", [P, M2, P])
        y = wd2[0:1, 1, :]

        unit_ps = [pb(f"unit_ps{i}", [P, B]) for i in range(2)]
        gram_ps = pb("gram_ps", [P, HALF_BLOCKS, P])
        l1_ps = pb("l1_ps", [P, M1, P])
        l2_ps = pb("l2_ps", [P, 4, P])

        rows_landed = [sem(f"rows_landed{r}") for r in range(RING)]
        ids_landed = sem("ids_landed")
        ids_all_landed = [sem(f"ids_all_landed{h}") for h in range((NH + 1) // 2)]
        dense_landed = sem("dense_landed")
        tbl_landed = [sem(f"tbl_landed{r}") for r in range(2)]
        w1_landed = sem("w1_landed")
        wd_landed = sem("wd_landed")
        w23_landed = sem("w23_landed")
        ident_zeroed = sem("ident_zeroed")
        ident_ready = sem("ident_ready")
        iota_ready = sem("iota_ready")
        row_no_ready = sem("row_no_ready")
        pads_zeroed = sem("pads_zeroed")
        pairs_zeroed = sem("pairs_zeroed")
        wd_ready = sem("wd_ready")
        group_read = sem("group_read")
        unit_ready = sem("unit_ready")
        hi_stored = sem("hi_stored")
        lo_stored = sem("lo_stored")
        tbl_hi_ready = sem("tbl_hi_ready")
        tbl_lo_ready = sem("tbl_lo_ready")
        tbl_used = sem("tbl_used")
        onehot_ready = sem("onehot_ready")
        onehot_used = sem("onehot_used")
        gram_ready = sem("gram_ready")
        pairs_act = sem("pairs_act")
        pairs_dve = sem("pairs_dve")
        l1_ready = sem("l1_ready")
        h1_stored = sem("h1_stored")
        l2_ready = sem("l2_ready")
        h2_stored = sem("h2_stored")
        l3_ready = sem("l3_ready")
        y_stored = sem("y_stored")
        out_written = sem("out_written")

        block = ctx.enter_context(nc.Block())

        def unit_out(store, step):
            kind, a, b = step
            if kind == "group":
                s = group_slots(b)
                return store[:, a * P:(a + 1) * P, s[0]:s[-1] + 1]
            return store[:, 0:B, IN_ROWS + a]

        def unit_in(step):
            kind, _, b = step
            ps = unit_ps[unit_of[step] % 2]
            if kind == "group":
                return ps[:, 0:len(group_slots(b)) * P].rearrange("p (k x) -> p x k", x=P)
            return ps[:, :]

        def before(h):
            return sum(depth[:h])

        def pair_copies(s_range, t, half):
            for s in s_range:
                for q in range(4):
                    n = len(range(q, PAIR_COLS, 4))
                    c0 = s * PAIR_COLS + q
                    src = gram_ps[32 * s:32 * s + FEATURES, :, c0:c0 + 4 * (n - 1) + 1:4]
                    lo = s * 32 + half * HALF_BLOCKS
                    dst = pairs[32 * q:32 * q + FEATURES, t % 2, 0:n, lo:lo + HALF_BLOCKS]
                    yield dst, src.rearrange("p x c -> p c x")

        @block.sync
        def _(sp):
            sp.dma_start(ids_sb[:, :, :], ids.rearrange("p (t f) -> p t f", t=TILES)).then_inc(ids_landed, 16)

            def load_table(h):
                n = depth[h]
                if h >= 2:
                    sp.wait_ge(tbl_lo_ready, h - 1)
                src = tables[ONEHOT[h]].rearrange("(p k) d -> p k d", k=n)
                even = TBL_P // 16 * 16
                sp.dma_start(tbl[0:even, h % 2, 0:n, :], src[0:even]).then_inc(tbl_landed[h % 2], 16)
                sp.dma_start(tbl[even:TBL_P, h % 2, 0:n, :], src[even:TBL_P]).then_inc(tbl_landed[h % 2], 16)

            def load_ids(m):
                n = min(2, NH - 2 * m)
                if 2 * m >= IDS_RING:
                    sp.wait_ge(onehot_ready, before(2 * m - IDS_RING + 2))
                at = 2 * m % IDS_RING
                sp.dma_start(ids_all[:, at:at + n, :],
                             ids_rows[2 * m:2 * m + n, :].rearrange("(a h) b -> a h b", a=1).broadcast_to((P, n, B)))\
                    .then_inc(ids_all_landed[m], 16)

            if NH:
                load_ids(0)
                load_table(0)
                load_table(1)
            sp.dma_start(dense_rows[:, :, :], dense.rearrange("(t p) d -> p t d", p=P)).then_inc(dense_landed, 16)
            for h in range(2, NH):
                if h % 2 == 0:
                    load_ids(h // 2)
                load_table(h)
            sp.dma_start(w1[:, :, :], w_pairs.rearrange("p (c n) -> p c n", n=H1)).then_inc(w1_landed, 16)
            sp.wait_ge(onehot_ready, before(NH))
            sp.dma_start(wd2[:, :, :], w_dense.rearrange("(a p) n -> p a n", p=P)).then_inc(wd_landed, 16)
            sp.dma_start(w2[:, :, :], w_top2.rearrange("(k p) n -> p k n", p=P)).then_inc(w23_landed, 16)
            sp.dma_start(columns_sb[:, :], columns).then_inc(w23_landed, 16)
            sp.wait_ge(y_stored, TILES)
            sp.dma_start(out.rearrange("(a b) n -> a (b n)", a=1), y[:, :]).then_inc(out_written, 16)
            sp.wait_ge(out_written, 16)

        @block.gpsimd
        def _(pool):
            nc.gpsimd.memset(ident[:, :], 0.0).then_inc(ident_zeroed, 1)
            nc.gpsimd.iota(row_no_i[:, 0, :], [[1, DEPTH]], base=0, channel_multiplier=8).then_inc(iota_ready, 1)
            nc.gpsimd.iota(row_no_i[:, 1, :], [[1, DEPTH]], base=0, channel_multiplier=10).then_inc(iota_ready, 1)
            pool.wait_ge(ident_zeroed, 1)
            nc.gpsimd.affine_select(out=ident[:, :], in_=ident[:, :], compare_op=ALU.not_equal, fill=1.0,
                                    base=0, pattern=[[-1, P]], channel_multiplier=1).then_inc(ident_ready, 1)
            pool.wait_ge(ids_landed, 16)
            for n in range(TILES * GROUPS):
                t, g = divmod(n, GROUPS)
                if n >= RING:
                    pool.wait_ge(group_read, n - RING + 1)
                for k, s in enumerate(group_slots(g)):
                    if s == 0:
                        continue
                    f = SLOTS[s] - 1
                    nc.gpsimd.indirect_dma_start(
                        out=rows[:, n % RING, k, :], out_offset=None, in_=tables[f],
                        in_offset=bass.IndirectOffsetOnAxis(ap=ids_sb[:, t, f:f + 1], axis=0),
                    ).then_inc(rows_landed[n % RING], 16)

        @block.scalar
        def _(act):
            def table_hi(h):
                if h >= NH:
                    return
                act.wait_ge(tbl_landed[h % 2], 32 * (h // 2 + 1))
                if h >= 2:
                    act.wait_ge(tbl_used, h - 1)
                n = depth[h]
                nc.scalar.activation(tbl_hi[0:TBL_P, h % 2, 0:n, :], tbl[0:TBL_P, h % 2, 0:n, :], ACT.Copy)\
                    .then_inc(tbl_hi_ready, 1)

            table_hi(0)
            for step in order:
                kind, a, b = step
                if kind in ("group", "onehot"):
                    if kind == "onehot":
                        table_hi(a + 1)
                    act.wait_ge(unit_ready, unit_of[step] + 1)
                    if kind == "group" and b == 0:
                        nc.scalar.activation(dense_t[:, a * P:(a + 1) * P].rearrange("p (s x) -> p s x", s=BLOCK),
                                             unit_ps[unit_of[step] % 2][:, 0:P].rearrange("p (x s) -> p s x", s=BLOCK), ACT.Copy)
                    nc.scalar.activation(unit_out(feat_hi, step), unit_in(step), ACT.Copy).then_inc(hi_stored, 1)
                elif kind == "gram":
                    act.wait_ge(gram_ready, 2 * a + b + 1)
                    if a == 0 and b == 0:
                        act.wait_ge(pairs_zeroed, 1)
                    if a >= 2:
                        act.wait_ge(l1_ready, a - 1)
                    for dst, src in pair_copies((0, 1), a, b):
                        last = nc.scalar.activation(dst, src, ACT.Copy)
                    last.then_inc(pairs_act, 1)
                elif kind == "l1":
                    act.wait_ge(l1_ready, a + 1)
                    if a == 0:
                        act.wait_ge(w23_landed, 32)
                    if a:
                        act.wait_ge(l2_ready, a)
                    for m in range(M1):
                        last = nc.scalar.activation(h1[:, m, :], l1_ps[:, m, :], ACT.Relu, bias=b1[:, m:m + 1])
                    last.then_inc(h1_stored, 1)

        @block.vector
        def _(dve):
            nc.vector.memset(feat_hi[:, :, FEATURES:PAD].bitcast(F32), 0.0)
            nc.vector.memset(feat_lo[:, :, FEATURES:PAD].bitcast(F32), 0.0).then_inc(pads_zeroed, 1)
            dve.wait_ge(iota_ready, 2)
            nc.vector.tensor_copy(row_no[:, :, :], row_no_i[:, :, :]).then_inc(row_no_ready, 1)

            def split_table(h):
                if h >= NH:
                    return
                n = depth[h]
                dve.wait_ge(tbl_hi_ready, h + 1)
                if h >= 2:
                    dve.wait_ge(tbl_used, h - 1)
                nc.vector.tensor_tensor(tbl_lo[0:TBL_P, h % 2, 0:n, :], tbl[0:TBL_P, h % 2, 0:n, :],
                                        tbl_hi[0:TBL_P, h % 2, 0:n, :].bitcast(F32), ALU.subtract).then_inc(tbl_lo_ready, 1)

            def onehot_tiles(h, first, end):
                if h >= NH:
                    return
                if first == 0 and h % 2 == 0:
                    dve.wait_ge(ids_all_landed[h // 2], 16)
                for k in range(first, min(end, depth[h])):
                    i = before(h) + k
                    if i >= OH_RING:
                        dve.wait_ge(onehot_used, i - OH_RING + 1)
                    nc.vector.tensor_scalar(onehot[0:TBL_P, i % OH_RING, :], ids_all[0:TBL_P, h % IDS_RING, :],
                                            row_no[0:TBL_P, int(depth[h] == 10), k:k + 1], None, ALU.is_equal)\
                        .then_inc(onehot_ready, 1)

            split_table(0)
            dve.wait_ge(row_no_ready, 1)
            onehot_tiles(0, 0, DEPTH)
            for step in order:
                kind, a, b = step
                if kind in ("group", "onehot"):
                    if kind == "onehot":
                        split_table(a + 1)
                        onehot_tiles(a + 1, 0, OH_RING)
                        if a == NH - 1:
                            dve.wait_ge(tbl_lo_ready, NH)
                            nc.vector.memset(pairs[:, :, :, :], 0.0).then_inc(pairs_zeroed, 1)
                    dve.wait_ge(hi_stored, unit_of[step] + 1)
                    nc.vector.tensor_tensor(unit_out(feat_lo, step), unit_in(step),
                                            unit_out(feat_hi, step).bitcast(F32), ALU.subtract).then_inc(lo_stored, 1)
                    if kind == "onehot":
                        onehot_tiles(a + 1, OH_RING, DEPTH)
                elif kind == "gram":
                    if a == 0 and b == 0:
                        dve.wait_ge(wd_landed, 16)
                        nc.vector.tensor_tensor(wd[:, :], wd2[:, 0, :], wd2[:, 1, :], ALU.add).then_inc(wd_ready, 1)
                        dve.wait_ge(pairs_zeroed, 1)
                    dve.wait_ge(gram_ready, 2 * a + b + 1)
                    if a >= 2:
                        dve.wait_ge(l1_ready, a - 1)
                    for dst, src in pair_copies((2, 3), a, b):
                        last = nc.vector.tensor_copy(dst, src)
                    last.then_inc(pairs_dve, 1)
                elif kind == "l2":
                    dve.wait_ge(l2_ready, a + 1)
                    if a == 0:
                        dve.wait_ge(w23_landed, 32)
                    else:
                        dve.wait_ge(l3_ready, a)
                    for m in range(M2):
                        last = nc.vector.tensor_scalar(h2[:, m, :], l2_ps[:, m, :], b2[:, m:m + 1], 0.0, ALU.add, ALU.max)
                    last.then_inc(h2_stored, 1)
                elif kind == "l3":
                    dve.wait_ge(l3_ready, a + 1)
                    nc.vector.tensor_copy(y[:, a * P:(a + 1) * P].rearrange("p (x s) -> p s x", s=BLOCK),
                                          l2_ps[0:1, M2, :].rearrange("p (s x) -> p s x", s=BLOCK)).then_inc(y_stored, 1)

        @block.tensor
        def _(pe):
            pe.wait_ge(ident_ready, 1)

            def bank_free(u):
                if u >= 2:
                    pe.wait_ge(lo_stored, u - 1)

            def group(t, g):
                n = t * GROUPS + g
                u = unit_of["group", t, g]
                bank_free(u)
                slots = group_slots(g)
                if g == 0 and t == 0:
                    pe.wait_ge(dense_landed, 16)
                count = len([s for s in slots if s])
                pe.wait_ge(rows_landed[n % RING], gather_count(n))
                for k, s in enumerate(slots):
                    src = dense_rows[:, t, :] if s == 0 else rows[:, n % RING, k, :]
                    last = nc.tensor.transpose(unit_ps[u % 2][:, k * P:(k + 1) * P], src, ident[:, :])
                last.then_inc(group_read, 1)
                pe.wait_ge(group_read, n + 1)
                pe.sem_inc(unit_ready, 1)

            def gather_count(n):
                return sum(16 * len([s for s in group_slots(m % GROUPS) if s]) for m in range(n % RING, n + 1, RING))

            def onehot_product(h):
                u = unit_of["onehot", h, 0]
                bank_free(u)
                pe.wait_ge(tbl_lo_ready, h + 1)
                n = depth[h]
                for k in range(n):
                    i = before(h) + k
                    pe.wait_ge(onehot_ready, i + 1)
                    nc.tensor.matmul(unit_ps[u % 2][:, :], tbl_hi[0:TBL_P, h % 2, k, :], onehot[0:TBL_P, i % OH_RING, :],
                                     start=(k == 0), stop=False)
                    last = nc.tensor.matmul(unit_ps[u % 2][:, :], tbl_lo[0:TBL_P, h % 2, k, :],
                                            onehot[0:TBL_P, i % OH_RING, :], start=False, stop=(k == n - 1))
                    last.then_inc(onehot_used, 1)
                pe.wait_ge(onehot_used, before(h) + n)
                pe.sem_inc(tbl_used, 1)
                pe.sem_inc(unit_ready, 1)

            def gram(t, half):
                if half == 0:
                    if t == 0:
                        pe.wait_ge(pads_zeroed, 1)
                    pe.wait_ge(lo_stored, last_unit[t] + 1)
                if t or half:
                    pe.wait_ge(pairs_act, 2 * t + half)
                    pe.wait_ge(pairs_dve, 2 * t + half)
                for x in range(HALF_BLOCKS):
                    b = t * P + (half * HALF_BLOCKS + x) * BLOCK

                    def still(store):
                        return store[:, b:b + BLOCK, :].rearrange("p s f -> p (s f)")

                    def moving(store):
                        return store[:, b:b + BLOCK, 1:FEATURES]

                    for n, (w, m) in enumerate([(feat_hi, feat_hi), (feat_hi, feat_lo), (feat_lo, feat_hi)]):
                        last = nc.tensor.matmul(gram_ps[:, x, 0:BLOCK * PAIR_COLS], still(w), moving(m),
                                                start=(n == 0), stop=(n == 2))
                last.then_inc(gram_ready, 1)

            def layer1(t):
                if t == 0:
                    pe.wait_ge(w1_landed, 16)
                    pe.wait_ge(wd_ready, 1)
                else:
                    pe.wait_ge(h1_stored, t)
                pe.wait_ge(pairs_act, 2 * t + 2)
                pe.wait_ge(pairs_dve, 2 * t + 2)
                for m in range(M1):
                    nc.tensor.matmul(l1_ps[:, m, :], wd[:, m * P:(m + 1) * P], dense_t[:, t * P:(t + 1) * P],
                                     start=True, stop=False)
                    for c in range(CHUNKS):
                        k = 32 * min(4, PAIR_COLS - 4 * c)
                        last = nc.tensor.matmul(l1_ps[:, m, :], w1[0:k, c, m * P:(m + 1) * P], pairs[0:k, t % 2, c, :],
                                                start=False, stop=(c == CHUNKS - 1))
                last.then_inc(l1_ready, 1)

            def layer2(t):
                pe.wait_ge(h1_stored, t + 1)
                if t == 0:
                    pe.wait_ge(w23_landed, 32)
                else:
                    pe.wait_ge(y_stored, t)
                for m in range(M2):
                    for k in range(M1):
                        last = nc.tensor.matmul(l2_ps[:, m, :], w2[:, k, m * P:(m + 1) * P], h1[:, k, :],
                                                start=(k == 0), stop=(k == M1 - 1))
                last.then_inc(l2_ready, 1)

            def layer3(t):
                pe.wait_ge(h2_stored, t + 1)
                for k in range(M2):
                    last = nc.tensor.matmul(l2_ps[0:1, M2, :], w3[:, k:k + 1], h2[:, k, :],
                                            start=(k == 0), stop=(k == M2 - 1))
                last.then_inc(l3_ready, 1)

            for kind, a, b in order:
                if kind == "group":
                    group(a, b)
                elif kind == "onehot":
                    onehot_product(a)
                elif kind == "gram":
                    gram(a, b)
                elif kind == "l1":
                    layer1(a)
                elif kind == "l2":
                    layer2(a)
                elif kind == "l3":
                    layer3(a)


def kernel(**inputs):
    import numpy as np
    from concourse import bacc
    from concourse.bass_utils import run_bass_kernel_spmd

    nc = bacc.Bacc("TRN2", target_bir_lowering=False, num_devices=1)
    arrays = {}

    def arg(name, a):
        a = np.ascontiguousarray(a)
        arrays[name] = a
        return nc.dram_tensor(name, a.shape, mybir.dt.from_np(a.dtype), kind="ExternalInput").ap()

    given = {k: np.asarray(v) for k, v in inputs.items()}
    B = given["ids"].shape[0]
    w_top1 = given["W_top1"]
    w_pairs = np.zeros((P, CHUNKS, H1), w_top1.dtype)
    for j in range(1, FEATURES):
        c, q = divmod(j - 1, 4)
        for i in range(j):
            w_pairs[32 * q + i, c] = w_top1[pair_row(SLOTS[i], SLOTS[j])]
    dense = arg("dense", given["r_dense_features"])
    ids = arg("ids", given["ids"].reshape(B // P, P, TABLES).transpose(1, 0, 2).reshape(P, -1))
    ids_rows = arg("ids_rows", given["ids"].T[ONEHOT])
    tables = [arg(f"tbl_{f}_dram", given[f"tbl_{f}"]) for f in range(TABLES)]
    args = [
        arg("w_pairs", w_pairs.reshape(P, -1)),
        arg("w_dense", np.concatenate([w_top1[:P], w_top1[-P:]])),
        arg("w_top2", given["W_top2"]),
        arg("columns", np.concatenate([given[k].reshape(-1, P).T for k in ("W_top3", "b_top1", "b_top2")], axis=1)),
    ]
    out = nc.dram_tensor("out", (B, 1), F32, kind="ExternalOutput").ap()
    dlrm_tower_kernel(nc, dense, ids, ids_rows, tables, *args, out)
    r = run_bass_kernel_spmd(nc, [arrays], core_ids=[0])
    return r.results[0]["out"]
```

```python
from contextlib import ExitStack

import concourse.bass as bass
from concourse import mybir

ALU = mybir.AluOpType
ACT = mybir.ActivationFunctionType
F32 = mybir.dt.float32
F32R = mybir.dt.float32r
I32 = mybir.dt.int32

P = 128
QUAD = 32
TABLES = 26
FEATURES = TABLES + 1
H1, H2 = 512, 256
M1, M2 = H1 // P, H2 // P

ONEHOT = [1, 7, 8, 9, 10, 11, 13, 14]
GATHERED = [f for f in range(TABLES) if f not in ONEHOT]
SLOTS = [0] + [f + 1 for f in GATHERED] + [f + 1 for f in ONEHOT] + [0]
DENSE_AGAIN = FEATURES
FIRST_ONEHOT = 1 + len(GATHERED)

PER_GROUP = 4
GROUPS = -(-len(GATHERED) // PER_GROUP)
RING = 8

TBL_P = 125
TBL_RING = 3
VEC_RING = 8
ACT_EVERY = 4
ACT_RING = 4

COUPLES = TABLES // 2
CHUNKS = -(-COUPLES // 4)
BLOCK = 4
PART = 8
PARTS = P // (PART * BLOCK)


def pair_row(a, b):
    i, j = min(a, b), max(a, b)
    return P + i * FEATURES - i * (i + 1) // 2 + j - i - 1


def takes_second(slot, u):
    if slot == 0 or slot == DENSE_AGAIN:
        return slot == DENSE_AGAIN
    v, second = divmod(slot - 1, 2)
    return bool(second) if v > u else not second


def pe_order(tiles):
    order = [("dense", 0, 0)]
    groups = [("group", t, g) for t in range(tiles) for g in range(GROUPS)]

    def take(n):
        for _ in range(min(n, len(groups))):
            order.append(groups.pop(0))

    for h in range(len(ONEHOT)):
        take(1)
        order.append(("onehot", h, 0))
    for t in range(tiles):
        while groups and groups[0][1] <= t:
            take(1)
        for k in range(PARTS):
            order.append(("gram", t, k))
            if t:
                order.append(("l1", t - 1, k))
            if k:
                take(1)
        if t:
            order += [("l2", t - 1, m) for m in range(M2)]
            take(1)
            order.append(("l3", t - 1, 0))
    order += [("l1", tiles - 1, m) for m in range(M1)]
    order += [("l2", tiles - 1, m) for m in range(M2)]
    order.append(("l3", tiles - 1, 0))
    return order


def dlrm_tower_kernel(nc, dense, ids, ids_rows, tables, w_pairs, w_dense, w_top2, columns, second, out):
    B = dense.shape[0]
    TILES = B // P
    NH = len(ONEHOT)
    DEPTH = tables[ONEHOT[0]].shape[0] // TBL_P

    order = pe_order(TILES)
    units = [s for s in order if s[0] in ("dense", "group", "onehot")]
    unit_of = {s: n for n, s in enumerate(units)}
    last_unit = [max([unit_of["group", t, g] for g in range(GROUPS)] +
                     [unit_of["onehot", h, 0] for h in range(NH)]) for t in range(TILES)]

    def by_act(k):
        return k % ACT_EVERY == ACT_EVERY - 1

    act_tiles = [k for k in range(DEPTH) if by_act(k)]
    vec_tiles = [k for k in range(DEPTH) if not by_act(k)]

    def group_tables(g):
        return range(g * PER_GROUP, min((g + 1) * PER_GROUP, len(GATHERED)))

    ctx = ExitStack()
    with ctx:
        def sb(name, shape, dt=F32):
            return ctx.enter_context(nc.sbuf_tensor(name, shape, dt))

        def pb(name, shape, dt=F32):
            return ctx.enter_context(nc.psum_tensor(name, shape, dt))

        def sem(name):
            return ctx.enter_context(nc.semaphore(name))

        feat = sb("feat", [P, B, QUAD])
        dense_rows = sb("dense_rows", [P, TILES, P])
        dense_t = sb("dense_t", [P, B])
        rows = sb("rows", [P, RING, PER_GROUP, P])
        ids_sb = sb("ids_sb", [P, TILES, TABLES], I32)
        ident = sb("ident", [P, P])

        ids_all = sb("ids_all", [P, NH, B], I32)
        row_no_i = sb("row_no_i", [P, DEPTH], I32)
        row_no = sb("row_no", [P, DEPTH])
        minus_row_no = sb("minus_row_no", [P, DEPTH])
        tbl = sb("tbl", [P, TBL_RING, DEPTH, P])
        tbl_hi = sb("tbl_hi", [P, TBL_RING, DEPTH, P], F32R)
        tbl_lo = sb("tbl_lo", [P, TBL_RING, DEPTH, P], F32R)
        vec_onehot = sb("vec_onehot", [P, VEC_RING, B], F32R)
        act_onehot = sb("act_onehot", [P, ACT_RING, B], F32R)
        distance = sb("distance", [P, B])

        w1 = sb("w1", [P, CHUNKS, H1])
        wd2 = sb("wd2", [P, 2, H1])
        wd = wd2[:, 0, :]
        y = wd2[0:1, 1, :]
        w2 = sb("w2", [P, M1, H2])
        columns_sb = sb("columns_sb", [P, M2 + M1 + M2])
        w3, b1, b2 = columns_sb[:, 0:M2], columns_sb[:, M2:M2 + M1], columns_sb[:, M2 + M1:]
        second_sb = sb("second_sb", [P, CHUNKS, PART], I32)
        pairs = sb("pairs", [P, 2, CHUNKS, P])
        h1 = sb("h1", [P, M1, P])
        h2 = sb("h2", [P, M2, P])

        unit_ps = [pb(f"unit_ps{i}", [P, B]) for i in range(2)]
        gram_ps = [pb(f"gram_ps{i}", [P, PART, P]) for i in range(2)]
        mlp_ps = [pb(f"mlp_ps{i}", [P, 4, P]) for i in range(2)]

        rows_landed = [sem(f"rows_landed{r}") for r in range(RING)]
        ids_landed = sem("ids_landed")
        ids_all_landed = [sem(f"ids_all_landed{w}") for w in range(NH // 2)]
        dense_landed = sem("dense_landed")
        tbl_landed = [sem(f"tbl_landed{r}") for r in range(TBL_RING)]
        w1_landed = sem("w1_landed")
        wd_landed = sem("wd_landed")
        w2_landed = sem("w2_landed")
        columns_landed = sem("columns_landed")
        second_landed = sem("second_landed")
        ident_zeroed = sem("ident_zeroed")
        ident_ready = sem("ident_ready")
        iota_ready = sem("iota_ready")
        row_no_ready = sem("row_no_ready")
        pads_zeroed = sem("pads_zeroed")
        pairs_zeroed = sem("pairs_zeroed")
        wd_ready = sem("wd_ready")
        group_read = sem("group_read")
        unit_ready = sem("unit_ready")
        unit_stored = sem("unit_stored")
        tbl_hi_ready = sem("tbl_hi_ready")
        tbl_lo_ready = sem("tbl_lo_ready")
        tbl_used = sem("tbl_used")
        vec_onehot_ready = sem("vec_onehot_ready")
        vec_onehot_used = sem("vec_onehot_used")
        distance_ready = sem("distance_ready")
        act_onehot_ready = sem("act_onehot_ready")
        act_onehot_used = sem("act_onehot_used")
        gram_ready = sem("gram_ready")
        first_stored = sem("first_stored")
        second_stored = sem("second_stored")
        l1_ready = sem("l1_ready")
        h1_stored = sem("h1_stored")
        l2_ready = sem("l2_ready")
        h2_stored = sem("h2_stored")
        l3_ready = sem("l3_ready")
        y_stored = sem("y_stored")
        out_written = sem("out_written")

        block = ctx.enter_context(nc.Block())

        def couple_parts(s, which, part, t):
            lo = s * QUAD + part * PART
            for q in range(4):
                n = len(range(q, COUPLES, 4))
                c0 = s * TABLES + 2 * q + which
                src = gram_ps[part % 2][QUAD * s:QUAD * s + FEATURES + 1, :, c0:c0 + 8 * (n - 1) + 1:8]
                dst = pairs[QUAD * q:QUAD * q + FEATURES + 1, t % 2, 0:n, lo:lo + PART]
                yield dst, src.rearrange("p x c -> p c x"), second_sb[QUAD * q:QUAD * q + FEATURES + 1, 0:n, :]

        @block.sync
        def _(sp):
            def load_table(h):
                if h >= TBL_RING:
                    sp.wait_ge(tbl_lo_ready, h - TBL_RING + 1)
                src = tables[ONEHOT[h]].rearrange("(p k) d -> p k d", k=DEPTH)
                even = TBL_P // 16 * 16
                sp.dma_start(tbl[0:even, h % TBL_RING, :, :], src[0:even]).then_inc(tbl_landed[h % TBL_RING], 16)
                sp.dma_start(tbl[even:TBL_P, h % TBL_RING, :, :], src[even:TBL_P]).then_inc(tbl_landed[h % TBL_RING], 16)

            def load_ids(w):
                sp.dma_start(ids_all[:, 2 * w:2 * w + 2, :],
                             ids_rows[2 * w:2 * w + 2, :].rearrange("(a h) b -> a h b", a=1).broadcast_to((P, 2, B)))\
                    .then_inc(ids_all_landed[w], 16)

            sp.dma_start(ids_sb[:, :, :], ids.rearrange("p (t f) -> p t f", t=TILES)).then_inc(ids_landed, 16)
            load_table(0)
            load_ids(0)
            load_table(1)
            sp.dma_start(dense_rows[:, :, :], dense.rearrange("(t p) d -> p t d", p=P)).then_inc(dense_landed, 16)
            for h in range(2, NH):
                if h % 2 == 0:
                    load_ids(h // 2)
                load_table(h)
            sp.dma_start(second_sb[:, :, :], second.rearrange("p (c x) -> p c x", c=CHUNKS)).then_inc(second_landed, 16)
            sp.dma_start(wd2[:, :, :], w_dense.rearrange("(a p) n -> p a n", p=P)).then_inc(wd_landed, 16)
            sp.dma_start(w1[:, :, :], w_pairs.rearrange("p (c n) -> p c n", n=H1)).then_inc(w1_landed, 16)
            sp.dma_start(w2[:, :, :], w_top2.rearrange("(k p) n -> p k n", p=P)).then_inc(w2_landed, 16)
            sp.dma_start(columns_sb[:, :], columns).then_inc(columns_landed, 16)
            sp.wait_ge(y_stored, TILES)
            sp.dma_start(out.rearrange("(a b) n -> a (b n)", a=1), y[:, :]).then_inc(out_written, 16)
            sp.wait_ge(out_written, 16)

        @block.gpsimd
        def _(pool):
            nc.gpsimd.memset(ident[:, :], 0.0).then_inc(ident_zeroed, 1)
            nc.gpsimd.iota(row_no_i[:, :], [[1, DEPTH]], base=0, channel_multiplier=DEPTH).then_inc(iota_ready, 1)
            pool.wait_ge(ident_zeroed, 1)
            nc.gpsimd.affine_select(out=ident[:, :], in_=ident[:, :], compare_op=ALU.not_equal, fill=1.0,
                                    base=0, pattern=[[-1, P]], channel_multiplier=1).then_inc(ident_ready, 1)
            pool.wait_ge(ids_landed, 16)
            for n in range(TILES * GROUPS):
                t, g = divmod(n, GROUPS)
                if n >= RING:
                    pool.wait_ge(group_read, n - RING + 1)
                for k, i in enumerate(group_tables(g)):
                    f = GATHERED[i]
                    nc.gpsimd.indirect_dma_start(
                        out=rows[:, n % RING, k, :], out_offset=None, in_=tables[f],
                        in_offset=bass.IndirectOffsetOnAxis(ap=ids_sb[:, t, f:f + 1], axis=0),
                    ).then_inc(rows_landed[n % RING], 16)

        @block.scalar
        def _(act):
            def table_hi(h):
                act.wait_ge(tbl_landed[h % TBL_RING], 32 * (h // TBL_RING + 1))
                if h >= TBL_RING:
                    act.wait_ge(tbl_used, h - TBL_RING + 1)
                nc.scalar.activation(tbl_hi[0:TBL_P, h % TBL_RING, :, :], tbl[0:TBL_P, h % TBL_RING, :, :], ACT.Copy)\
                    .then_inc(tbl_hi_ready, 1)

            def onehot_tiles(h):
                if h == 0:
                    act.wait_ge(row_no_ready, 2)
                act.wait_ge(ids_all_landed[h // 2], 16)
                for j, k in enumerate(act_tiles):
                    i = h * len(act_tiles) + j
                    if i:
                        act.wait_ge(act_onehot_ready, i)
                    nc.scalar.activation(distance[0:TBL_P, :], ids_all[0:TBL_P, h, :], ACT.Square,
                                         bias=minus_row_no[0:TBL_P, k:k + 1]).then_inc(distance_ready, 1)
                    if i >= ACT_RING:
                        act.wait_ge(act_onehot_used, i - ACT_RING + 1)
                    act.wait_ge(distance_ready, i + 1)
                    nc.scalar.activation(act_onehot[0:TBL_P, i % ACT_RING, :], distance[0:TBL_P, :], ACT.Relu,
                                         bias=1.0, scale=-1.0).then_inc(act_onehot_ready, 1)

            table_hi(0)
            onehot_tiles(0)
            for step in order:
                kind, a, b = step
                if kind == "onehot" and a + 1 < NH:
                    table_hi(a + 1)
                    onehot_tiles(a + 1)
                if kind in ("dense", "group", "onehot"):
                    ps = unit_ps[unit_of[step] % 2]
                    act.wait_ge(unit_ready, unit_of[step] + 1)
                    if kind == "dense":
                        nc.scalar.activation(dense_t[:, :].rearrange("p (t s x) -> p t s x", t=TILES, s=BLOCK),
                                             ps[:, :].rearrange("p (t x s) -> p t s x", t=TILES, s=BLOCK), ACT.Copy)
                        nc.scalar.activation(feat[:, :, 0], ps[:, :], ACT.Copy)
                        last = nc.scalar.activation(feat[:, :, DENSE_AGAIN], ps[:, :], ACT.Copy)
                    elif kind == "group":
                        n, s = len(group_tables(b)), 1 + group_tables(b)[0]
                        last = nc.scalar.activation(feat[:, a * P:(a + 1) * P, s:s + n],
                                                    ps[:, 0:n * P].rearrange("p (k x) -> p x k", x=P), ACT.Copy)
                    else:
                        last = nc.scalar.activation(feat[:, :, FIRST_ONEHOT + a], ps[:, :], ACT.Copy)
                    last.then_inc(unit_stored, 1)
                elif kind == "gram":
                    act.wait_ge(gram_ready, PARTS * a + b + 1)
                    if a == 0 and b == 0:
                        act.wait_ge(pairs_zeroed, 1)
                    if a >= 2 and b == 0:
                        act.wait_ge(l1_ready, M1 * (a - 1))
                    for s in range(4):
                        for dst, src, _ in couple_parts(s, 0, b, a):
                            last = nc.scalar.activation(dst, src, ACT.Copy)
                        last.then_inc(first_stored, 1)
                elif kind == "l1":
                    act.wait_ge(l1_ready, M1 * a + b + 1)
                    if a == 0 and b == 0:
                        act.wait_ge(columns_landed, 16)
                    if a and b == 0:
                        act.wait_ge(l2_ready, M2 * a)
                    nc.scalar.activation(h1[:, b, :], mlp_ps[b % 2][:, 0, :], ACT.Relu, bias=b1[:, b:b + 1])\
                        .then_inc(h1_stored, 1)
                elif kind == "l2":
                    act.wait_ge(l2_ready, M2 * a + b + 1)
                    if a and b == 0:
                        act.wait_ge(l3_ready, a)
                    nc.scalar.activation(h2[:, b, :], mlp_ps[b % 2][:, 1, :], ACT.Relu, bias=b2[:, b:b + 1])\
                        .then_inc(h2_stored, 1)
                elif kind == "l3":
                    act.wait_ge(l3_ready, a + 1)
                    if a == 0:
                        act.wait_ge(wd_ready, 1)
                    nc.scalar.activation(y[:, a * P:(a + 1) * P].rearrange("p (x s) -> p s x", s=BLOCK),
                                         mlp_ps[0][0:1, 2, :].rearrange("p (s x) -> p s x", s=BLOCK), ACT.Copy)\
                        .then_inc(y_stored, 1)

        @block.vector
        def _(dve):
            dve.wait_ge(iota_ready, 1)
            nc.vector.tensor_copy(row_no[:, :], row_no_i[:, :]).then_inc(row_no_ready, 1)
            nc.vector.tensor_scalar(minus_row_no[:, :], row_no_i[:, :], -1.0, None, ALU.mult).then_inc(row_no_ready, 1)
            nc.vector.memset(pairs[:, :, :, :], 0.0).then_inc(pairs_zeroed, 1)
            dve.wait_ge(row_no_ready, 2)
            for h in range(NH):
                dve.wait_ge(tbl_hi_ready, h + 1)
                if h >= TBL_RING:
                    dve.wait_ge(tbl_used, h - TBL_RING + 1)
                nc.vector.tensor_tensor(tbl_lo[0:TBL_P, h % TBL_RING, :, :], tbl[0:TBL_P, h % TBL_RING, :, :],
                                        tbl_hi[0:TBL_P, h % TBL_RING, :, :].bitcast(F32), ALU.subtract)\
                    .then_inc(tbl_lo_ready, 1)
                dve.wait_ge(ids_all_landed[h // 2], 16)
                for j, k in enumerate(vec_tiles):
                    i = h * len(vec_tiles) + j
                    if i >= VEC_RING:
                        dve.wait_ge(vec_onehot_used, i - VEC_RING + 1)
                    nc.vector.tensor_scalar(vec_onehot[0:TBL_P, i % VEC_RING, :], ids_all[0:TBL_P, h, :],
                                            row_no[0:TBL_P, k:k + 1], None, ALU.is_equal).then_inc(vec_onehot_ready, 1)
                if h == 0:
                    nc.vector.memset(feat[:, :, FEATURES + 1:QUAD], 0.0).then_inc(pads_zeroed, 1)
            dve.wait_ge(wd_landed, 16)
            nc.vector.tensor_tensor(wd[:, :], wd2[:, 0, :], wd2[:, 1, :], ALU.add).then_inc(wd_ready, 1)
            dve.wait_ge(second_landed, 16)
            for t in range(TILES):
                for part in range(PARTS):
                    for s in range(4):
                        dve.wait_ge(first_stored, 4 * (PARTS * t + part) + s + 1)
                        for dst, src, mask in couple_parts(s, 1, part, t):
                            last = nc.vector.copy_predicated(dst, mask, src)
                    last.then_inc(second_stored, 1)

        @block.tensor
        def _(pe):
            pe.wait_ge(ident_ready, 1)

            def bank(step):
                u = unit_of[step]
                if u >= 2:
                    pe.wait_ge(unit_stored, u - 1)
                return unit_ps[u % 2]

            def dense_unit():
                pe.wait_ge(dense_landed, 16)
                ps = bank(("dense", 0, 0))
                for t in range(TILES):
                    last = nc.tensor.transpose(ps[:, t * P:(t + 1) * P], dense_rows[:, t, :], ident[:, :])
                last.then_inc(unit_ready, 1)

            def group(t, g):
                n = t * GROUPS + g
                ps = bank(("group", t, g))
                pe.wait_ge(rows_landed[n % RING],
                           sum(16 * len(group_tables(m % GROUPS)) for m in range(n % RING, n + 1, RING)))
                for k in range(len(group_tables(g))):
                    last = nc.tensor.transpose(ps[:, k * P:(k + 1) * P], rows[:, n % RING, k, :], ident[:, :])
                last.then_inc(unit_ready, 1)
                pe.wait_ge(unit_ready, unit_of["group", t, g] + 1)
                pe.sem_inc(group_read, 1)

            def onehot_product(h):
                ps = bank(("onehot", h, 0))
                pe.wait_ge(tbl_lo_ready, h + 1)
                for k in range(DEPTH):
                    if by_act(k):
                        i = h * len(act_tiles) + act_tiles.index(k)
                        pe.wait_ge(act_onehot_ready, i + 1)
                        tile, used = act_onehot[0:TBL_P, i % ACT_RING, :], act_onehot_used
                    else:
                        i = h * len(vec_tiles) + vec_tiles.index(k)
                        pe.wait_ge(vec_onehot_ready, i + 1)
                        tile, used = vec_onehot[0:TBL_P, i % VEC_RING, :], vec_onehot_used
                    nc.tensor.matmul(ps[:, :], tbl_hi[0:TBL_P, h % TBL_RING, k, :], tile, start=(k == 0), stop=False)
                    nc.tensor.matmul(ps[:, :], tbl_lo[0:TBL_P, h % TBL_RING, k, :], tile,
                                     start=False, stop=(k == DEPTH - 1)).then_inc(used, 1)
                pe.wait_ge(used, i + 1)
                pe.sem_inc(tbl_used, 1)
                pe.sem_inc(unit_ready, 1)

            def gram(t, part):
                n = PARTS * t + part
                if part == 0:
                    if t == 0:
                        pe.wait_ge(pads_zeroed, 1)
                    pe.wait_ge(unit_stored, last_unit[t] + 1)
                if n >= 2:
                    pe.wait_ge(second_stored, n - 1)
                for x in range(PART):
                    b = t * P + (part * PART + x) * BLOCK
                    last = nc.tensor.matmul(gram_ps[part % 2][:, x, 0:BLOCK * TABLES],
                                            feat[:, b:b + BLOCK, :].rearrange("p s f -> p (s f)"),
                                            feat[:, b:b + BLOCK, 1:FEATURES], start=True, stop=True)
                last.then_inc(gram_ready, 1)

            def layer1(t, m):
                if t == 0 and m == 0:
                    pe.wait_ge(w1_landed, 16)
                    pe.wait_ge(wd_ready, 1)
                if m == 0:
                    pe.wait_ge(second_stored, PARTS * (t + 1))
                    if t:
                        pe.wait_ge(y_stored, t)
                if m >= 2:
                    pe.wait_ge(h1_stored, M1 * t + m - 1)
                ps = mlp_ps[m % 2][:, 0, :]
                nc.tensor.matmul(ps, wd[:, m * P:(m + 1) * P], dense_t[:, t * P:(t + 1) * P], start=True, stop=False)
                for c in range(CHUNKS):
                    k = QUAD * min(4, COUPLES - 4 * c)
                    last = nc.tensor.matmul(ps, w1[0:k, c, m * P:(m + 1) * P], pairs[0:k, t % 2, c, :],
                                            start=False, stop=(c == CHUNKS - 1))
                last.then_inc(l1_ready, 1)

            def layer2(t, m):
                if t == 0 and m == 0:
                    pe.wait_ge(w2_landed, 16)
                pe.wait_ge(h1_stored, M1 * (t + 1))
                for k in range(M1):
                    last = nc.tensor.matmul(mlp_ps[m % 2][:, 1, :], w2[:, k, m * P:(m + 1) * P], h1[:, k, :],
                                            start=(k == 0), stop=(k == M1 - 1))
                last.then_inc(l2_ready, 1)

            def layer3(t):
                pe.wait_ge(h2_stored, M2 * (t + 1))
                for k in range(M2):
                    last = nc.tensor.matmul(mlp_ps[0][0:1, 2, :], w3[:, k:k + 1], h2[:, k, :],
                                            start=(k == 0), stop=(k == M2 - 1))
                last.then_inc(l3_ready, 1)

            for kind, a, b in order:
                if kind == "dense":
                    dense_unit()
                elif kind == "group":
                    group(a, b)
                elif kind == "onehot":
                    onehot_product(a)
                elif kind == "gram":
                    gram(a, b)
                elif kind == "l1":
                    layer1(a, b)
                elif kind == "l2":
                    layer2(a, b)
                elif kind == "l3":
                    layer3(a)


def kernel(**inputs):
    import numpy as np
    from concourse import bacc
    from concourse.bass_utils import run_bass_kernel_spmd

    nc = bacc.Bacc("TRN2", target_bir_lowering=False, num_devices=1)
    arrays = {}

    def arg(name, a):
        a = np.ascontiguousarray(a)
        arrays[name] = a
        return nc.dram_tensor(name, a.shape, mybir.dt.from_np(a.dtype), kind="ExternalInput").ap()

    given = {k: np.asarray(v) for k, v in inputs.items()}
    B = given["ids"].shape[0]
    w_top1 = given["W_top1"]
    w_pairs = np.zeros((P, CHUNKS, H1), w_top1.dtype)
    second = np.zeros((P, CHUNKS, PART), np.int32)
    for u in range(COUPLES):
        c, q = divmod(u, 4)
        for slot in range(FEATURES + 1):
            other = 1 + 2 * u + int(takes_second(slot, u))
            second[QUAD * q + slot, c] = takes_second(slot, u)
            if slot != 2 + 2 * u:
                w_pairs[QUAD * q + slot, c] = w_top1[pair_row(SLOTS[slot], SLOTS[other])]
    dense = arg("dense", given["r_dense_features"])
    ids = arg("ids", given["ids"].reshape(B // P, P, TABLES).transpose(1, 0, 2).reshape(P, -1))
    ids_rows = arg("ids_rows", given["ids"].T[ONEHOT])
    tables = [arg(f"tbl_{f}_dram", given[f"tbl_{f}"]) for f in range(TABLES)]
    args = [
        arg("w_pairs", w_pairs.reshape(P, -1)),
        arg("w_dense", np.concatenate([w_top1[:P], w_top1[-P:]])),
        arg("w_top2", given["W_top2"]),
        arg("columns", np.concatenate([given[k].reshape(-1, P).T for k in ("W_top3", "b_top1", "b_top2")], axis=1)),
        arg("second", second.reshape(P, -1)),
    ]
    out = nc.dram_tensor("out", (B, 1), F32, kind="ExternalOutput").ap()
    dlrm_tower_kernel(nc, dense, ids, ids_rows, tables, *args, out)
    r = run_bass_kernel_spmd(nc, [arrays], core_ids=[0])
    return r.results[0]["out"]
```

```python
from contextlib import ExitStack

import concourse.bass as bass
from concourse import mybir

ALU = mybir.AluOpType
ACT = mybir.ActivationFunctionType
F32 = mybir.dt.float32
F32R = mybir.dt.float32r
I32 = mybir.dt.int32

P = 128
QUAD = 32
TABLES = 26
FEATURES = TABLES + 1
H1, H2 = 512, 256
M1, M2 = H1 // P, H2 // P

FULL = [1, 7, 8, 9, 10, 11, 13, 14]
LATE = [15]
LATE_TILE = 2
ONEHOT = FULL + LATE
GATHERED = [f for f in range(TABLES) if f not in ONEHOT] + LATE
SLOTS = [0] + [f + 1 for f in GATHERED] + [f + 1 for f in FULL[2:] + FULL[:2]]
COUPLES = (FEATURES - 3) // 2
LOOSE = [0, 2 * COUPLES + 1, 2 * COUPLES + 2]
SLOTS += [SLOTS[s] for s in LOOSE] + [SLOTS[LOOSE[0]], SLOTS[LOOSE[2]]]


PER_GROUP = 4
RING = 8

TBL_P = 125
TBL_RING = 3
VEC_RING = 8
ACT_EVERY = 5
ACT_RING = 4

LENGTH = {"dense": 4, "onehot": 35, "late": 4.3, "group": 4.3, "gram": 17.5, "l1": 8.7, "l2": 8.7, "l3": 5}
GATHER = 10.4
START = 59
LANDING = 45
CROWD = 30
LEFT = [5, 3, 2, 0]
LEFT_LAST = [2, 1, 1, 0]
LATE_STEPS = 4
WARM_UP = 10

CHUNKS = COUPLES // 4
BLOCK = 4
PART = 8
PARTS = P // (PART * BLOCK)


def onehot_slot(h):
    return SLOTS.index(ONEHOT[h] + 1)


def gathered(t):
    return len(GATHERED) - (len(LATE) if t >= LATE_TILE else 0)


def group_tables(t, g):
    return range(g * PER_GROUP, min((g + 1) * PER_GROUP, gathered(t)))


def tile_groups(t):
    return [("group", t, g) for g in range(-(-gathered(t) // PER_GROUP))]


def pair_row(a, b):
    i, j = min(a, b), max(a, b)
    return P + i * FEATURES - i * (i + 1) // 2 + j - i - 1


def takes_second(slot, u):
    if slot in LOOSE or slot >= FEATURES:
        return FEATURES <= slot < FEATURES + len(LOOSE)
    v, second = divmod(slot - 1, 2)
    return bool(second) if v > u else not second


def pair_of_row(slot, u):
    if slot >= FEATURES + len(LOOSE):
        a = LOOSE[0] if slot == QUAD - 2 else LOOSE[2]
        b = {0: LOOSE[1], 4: LOOSE[2]}.get(u, a)
    else:
        a, b = slot, 1 + 2 * u + int(takes_second(slot, u))
    return None if SLOTS[a] == SLOTS[b] or slot == 2 + 2 * u else (a, b)


def pe_order(tiles):
    order, clock = [], START
    groups = [step for t in range(tiles) for step in tile_groups(t)]
    landing, at = {}, LANDING
    for step in groups:
        at += GATHER * len(group_tables(*step[1:]))
        landing[step] = at + (CROWD if step[1] == 0 else 0)

    def run(step):
        nonlocal clock
        order.append(step)
        clock += LENGTH[step[0]]
        while groups and landing[groups[0]] <= clock:
            order.append(groups.pop(0))
            clock += LENGTH["group"]

    for h in range(len(FULL)):
        run(("onehot", h, 0))
        if h == 0:
            run(("dense", 0, 0))
    layers = []
    for t in range(tiles):
        while len(layers) > M2 + 1 and landing[tile_groups(t)[-1]] > clock:
            run(layers.pop(0))
        if t == 0:
            order.extend(("late", h, 0) for h in range(len(FULL), len(ONEHOT)))
        while groups and groups[0][1] <= t:
            clock = max(clock, landing[groups[0]])
            run(groups.pop(0))
        if t > 1 and order[-1][0] == "group":
            run(layers.pop(0))
        for k in range(PARTS):
            run(("gram", t, k))
            if t == 0 and k + 1 < LATE_STEPS:
                for h in range(len(FULL), len(ONEHOT)):
                    run(("late", h, k + 1))
            while layers and len(layers) > (LEFT_LAST if t == tiles - 1 else LEFT)[k]:
                run(layers.pop(0))
        last_l3 = [("l3", t - 1, 0)] if t else []
        layers = last_l3 + [("l1", t, m) for m in range(M1)] + [("l2", t, m) for m in range(M2)]
    for step in layers + [("l3", tiles - 1, 0)]:
        run(step)
    return order


def dlrm_tower_kernel(nc, dense, ids, ids_rows, tables, w_pairs, w_dense, w_top2, columns, masks, out):
    B = dense.shape[0]
    TILES = B // P
    NH = len(ONEHOT)
    DEPTH = tables[ONEHOT[0]].shape[0] // TBL_P

    assert all(tables[f].shape[0] == DEPTH * TBL_P for f in ONEHOT)
    assert LATE_STEPS <= PARTS and B * 4 <= 2048

    order = pe_order(TILES)
    units = [s for s in order if s[0] in ("dense", "group", "l3")]
    unit_of = {s: n for n, s in enumerate(units)}

    act_tiles = [n for n in range(NH * DEPTH) if n % ACT_EVERY == ACT_EVERY - 1]
    vec_tiles = [n for n in range(NH * DEPTH) if n % ACT_EVERY != ACT_EVERY - 1]

    groups = [step for t in range(TILES) for step in tile_groups(t)]

    def columns_of(h):
        return slice(0 if h < len(FULL) else LATE_TILE * P, B)

    ctx = ExitStack()
    with ctx:
        def sb(name, shape, dt=F32):
            return ctx.enter_context(nc.sbuf_tensor(name, shape, dt))

        def pb(name, shape, dt=F32):
            return ctx.enter_context(nc.psum_tensor(name, shape, dt))

        def sem(name):
            return ctx.enter_context(nc.semaphore(name))

        feat = sb("feat", [P, B, QUAD])
        dense_rows = sb("dense_rows", [P, TILES, P])
        dense_t = sb("dense_t", [P, B])
        rows = sb("rows", [P, RING, PER_GROUP, P])
        ids_sb = sb("ids_sb", [P, TILES, TABLES], I32)
        ident = sb("ident", [P, P])

        ids_all = sb("ids_all", [P, NH, B], I32)
        row_no_i = sb("row_no_i", [P, DEPTH], I32)
        row_no = sb("row_no", [P, DEPTH])
        minus_row_no = sb("minus_row_no", [P, DEPTH])
        tbl = sb("tbl", [P, TBL_RING, DEPTH, P])
        tbl_hi = sb("tbl_hi", [P, TBL_RING, DEPTH, P], F32R)
        tbl_lo = sb("tbl_lo", [P, TBL_RING, DEPTH, P], F32R)
        vec_onehot = sb("vec_onehot", [P, VEC_RING, B], F32R)
        act_onehot = sb("act_onehot", [P, ACT_RING, B], F32R)
        distance = sb("distance", [P, 2, B])

        w1 = sb("w1", [P, CHUNKS, H1])
        wd2 = sb("wd2", [P, 2, H1])
        wd = wd2[:, 0, :]
        y = wd2[0:1, 1, :]
        w2 = sb("w2", [P, M1, H2])
        columns_sb = sb("columns_sb", [P, M2 + M1 + M2])
        w3, b1, b2 = columns_sb[:, 0:M2], columns_sb[:, M2:M2 + M1], columns_sb[:, M2 + M1:]
        masks_sb = sb("masks_sb", [P, CHUNKS + 2, PART], I32)
        pairs = sb("pairs", [P, 2, CHUNKS, P])
        h1 = sb("h1", [P, M1, P])
        h2 = sb("h2", [P, M2, P])

        unit_ps = [pb(f"unit_ps{i}", [P, B]) for i in range(2)]
        gram_ps = [pb(f"gram_ps{i}", [P, PART, P]) for i in range(2)]
        mlp_ps = [pb(f"mlp_ps{i}", [P, 4, P]) for i in range(2)]

        rows_landed = [sem(f"rows_landed{r}") for r in range(RING)]
        ids_landed = sem("ids_landed")
        ids_all_landed = [sem(f"ids_all_landed{h}") for h in range(NH)]
        dense_landed = sem("dense_landed")
        tbl_start_landed = sem("tbl_start_landed")
        tbl_landed = [sem(f"tbl_landed{r}") for r in range(TBL_RING)]
        w1_landed = sem("w1_landed")
        wd_landed = sem("wd_landed")
        w2_landed = sem("w2_landed")
        columns_landed = sem("columns_landed")
        masks_landed = sem("masks_landed")
        ident_zeroed = sem("ident_zeroed")
        ident_ready = sem("ident_ready")
        iota_ready = sem("iota_ready")
        row_no_ready = sem("row_no_ready")
        repeats_stored = sem("repeats_stored")
        wd_ready = sem("wd_ready")
        unit_ready = sem("unit_ready")
        unit_stored = sem("unit_stored")
        product_ready = sem("product_ready")
        product_stored = sem("product_stored")
        tbl_hi_ready = sem("tbl_hi_ready")
        tbl_lo_ready = sem("tbl_lo_ready")
        vec_onehot_ready = sem("vec_onehot_ready")
        vec_onehot_used = sem("vec_onehot_used")
        distance_ready = sem("distance_ready")
        act_onehot_ready = sem("act_onehot_ready")
        act_onehot_used = sem("act_onehot_used")
        gram_ready = sem("gram_ready")
        first_stored = sem("first_stored")
        quadrant_stored = sem("quadrant_stored")
        second_stored = sem("second_stored")
        l1_ready = sem("l1_ready")
        h1_stored = sem("h1_stored")
        l2_ready = sem("l2_ready")
        h2_stored = sem("h2_stored")
        out_written = sem("out_written")

        block = ctx.enter_context(nc.Block())

        def halves(h):
            return [slice(0, DEPTH // 2), slice(DEPTH // 2, DEPTH)] if h == 0 else [slice(0, DEPTH)]

        def released(tiles, i, used):
            if tiles[i] % DEPTH == DEPTH - 1:
                return product_ready, tiles[i] // DEPTH + 1
            return used, sum(n % DEPTH != DEPTH - 1 for n in tiles[:i + 1])

        def product_bank(h):
            n = B // P if h < len(FULL) else B // P - LATE_TILE
            return (gram_ps if h < len(FULL) else mlp_ps)[h % 2][:, 0:n, :].rearrange("p a x -> p (a x)")

        def couple_parts(s, which, part, t):
            lo = s * QUAD + part * PART
            for q in range(4):
                c0 = s * TABLES + 2 * q + which
                src = gram_ps[part % 2][QUAD * s:QUAD * (s + 1), :, c0:c0 + 8 * (CHUNKS - 1) + 1:8]
                dst = pairs[QUAD * q:QUAD * (q + 1), t % 2, :, lo:lo + PART]
                yield dst, src.rearrange("p x c -> p c x"), masks_sb[QUAD * q:QUAD * (q + 1), 0:CHUNKS, :]

        def loose_part(s, part, t):
            lo = s * QUAD + part * PART
            c0 = s * TABLES + LOOSE[1] - 1
            src = gram_ps[part % 2][QUAD * s:QUAD * (s + 1), :, c0:c0 + 2]
            return (pairs[0:QUAD, t % 2, 0:2, lo:lo + PART], masks_sb[0:QUAD, CHUNKS:CHUNKS + 2, :],
                    src.rearrange("p x c -> p c x"))

        @block.sync
        def _(sp):
            def load_table(h, ks, landed):
                if h >= TBL_RING:
                    sp.wait_ge(tbl_lo_ready, h - TBL_RING + 2)
                src = tables[ONEHOT[h]].rearrange("(p k) d -> p k d", k=DEPTH)
                even = TBL_P // 16 * 16
                sp.dma_start(tbl[0:even, h % TBL_RING, ks, :], src[0:even, ks]).then_inc(landed, 16)
                sp.dma_start(tbl[even:TBL_P, h % TBL_RING, ks, :], src[even:TBL_P, ks]).then_inc(landed, 16)

            def load_ids(h):
                sp.dma_start(ids_all[:, h, :], ids_rows[h:h + 1, :].broadcast_to((P, B)))\
                    .then_inc(ids_all_landed[h], 16)

            sp.dma_start(ids_sb[:, :, :], ids.rearrange("p (t f) -> p t f", t=TILES)).then_inc(ids_landed, 16)
            load_table(0, halves(0)[0], tbl_start_landed)
            load_ids(0)
            load_table(0, halves(0)[1], tbl_landed[0])
            load_table(1, halves(1)[0], tbl_landed[1])
            load_ids(1)
            sp.dma_start(dense_rows[:, :, :], dense.rearrange("(t p) d -> p t d", p=P)).then_inc(dense_landed, 16)
            for h in range(2, NH):
                load_table(h, halves(h)[0], tbl_landed[h % TBL_RING])
                load_ids(h)
            sp.dma_start(masks_sb[:, :, :], masks.rearrange("p (c x) -> p c x", x=PART)).then_inc(masks_landed, 16)
            sp.dma_start(wd2[:, :, :], w_dense.rearrange("(a p) n -> p a n", p=P)).then_inc(wd_landed, 16)
            sp.wait_ge(product_ready, len(FULL) - 2)
            for c in range(CHUNKS):
                sp.dma_start(w1[:, c, :], w_pairs[:, c * H1:(c + 1) * H1]).then_inc(w1_landed, 16)
            sp.dma_start(w2[:, :, :], w_top2.rearrange("(k p) n -> p k n", p=P)).then_inc(w2_landed, 16)
            sp.dma_start(columns_sb[:, :], columns).then_inc(columns_landed, 16)
            sp.wait_ge(unit_stored, len(units))
            sp.dma_start(out.rearrange("(a b) n -> a (b n)", a=1), y[:, :]).then_inc(out_written, 16)
            sp.wait_ge(out_written, 16)

        @block.gpsimd
        def _(pool):
            nc.gpsimd.memset(ident[:, :], 0.0).then_inc(ident_zeroed, 1)
            nc.gpsimd.iota(row_no_i[:, :], [[1, DEPTH]], base=0, channel_multiplier=DEPTH).then_inc(iota_ready, 1)
            pool.wait_ge(ident_zeroed, 1)
            nc.gpsimd.affine_select(out=ident[:, :], in_=ident[:, :], compare_op=ALU.not_equal, fill=1.0,
                                    base=0, pattern=[[-1, P]], channel_multiplier=1).then_inc(ident_ready, 1)
            pool.wait_ge(ids_landed, 16)
            for n, (_, t, g) in enumerate(groups):
                if n >= RING:
                    pool.wait_ge(unit_ready, unit_of[groups[n - RING]] + 1)
                for k, i in enumerate(group_tables(t, g)):
                    f = GATHERED[i]
                    nc.gpsimd.indirect_dma_start(
                        out=rows[:, n % RING, k, :], out_offset=None, in_=tables[f],
                        in_offset=bass.IndirectOffsetOnAxis(ap=ids_sb[:, t, f:f + 1], axis=0),
                    ).then_inc(rows_landed[n % RING], 16)

        @block.scalar
        def _(act):
            def table_hi(h):
                if h >= TBL_RING:
                    act.wait_ge(product_ready, h - TBL_RING + 1)
                for ks in halves(h):
                    if ks.stop < DEPTH:
                        act.wait_ge(tbl_start_landed, 32)
                    else:
                        act.wait_ge(tbl_landed[h % TBL_RING], 32 * (h // TBL_RING + 1))
                    nc.scalar.activation(tbl_hi[0:TBL_P, h % TBL_RING, ks, :], tbl[0:TBL_P, h % TBL_RING, ks, :],
                                         ACT.Copy).then_inc(tbl_hi_ready, 1)

            def onehot_tiles(h):
                if h == 0:
                    act.wait_ge(row_no_ready, 2)
                act.wait_ge(ids_all_landed[h], 16)
                cols = columns_of(h)
                mine = [(i, n % DEPTH) for i, n in enumerate(act_tiles) if n // DEPTH == h]
                for i, k in mine:
                    if i >= 2:
                        act.wait_ge(act_onehot_ready, i - 1)
                    nc.scalar.activation(distance[0:TBL_P, i % 2, cols], ids_all[0:TBL_P, h, cols], ACT.Square,
                                         bias=minus_row_no[0:TBL_P, k:k + 1]).then_inc(distance_ready, 1)
                for i, k in mine:
                    if i >= ACT_RING:
                        act.wait_ge(*released(act_tiles, i - ACT_RING, act_onehot_used))
                    act.wait_ge(distance_ready, i + 1)
                    nc.scalar.activation(act_onehot[0:TBL_P, i % ACT_RING, cols], distance[0:TBL_P, i % 2, cols],
                                         ACT.Relu, bias=1.0, scale=-1.0).then_inc(act_onehot_ready, 1)

            table_hi(0)
            onehot_tiles(0)
            table_hi(1)
            for step in order:
                kind, a, b = step
                if kind == "onehot" and a + 1 < NH:
                    onehot_tiles(a + 1)
                    if a + 2 < NH:
                        table_hi(a + 2)
                if kind == "onehot" or kind == "late" and b == LATE_STEPS - 1:
                    act.wait_ge(product_ready, a + 1)
                    nc.scalar.activation(feat[:, columns_of(a), onehot_slot(a)], product_bank(a), ACT.Copy)\
                        .then_inc(product_stored, 1)
                elif kind in ("dense", "group"):
                    ps = unit_ps[unit_of[step] % 2]
                    act.wait_ge(unit_ready, unit_of[step] + 1)
                    if kind == "dense":
                        nc.scalar.activation(dense_t[:, :].rearrange("p (t s x) -> p t s x", t=TILES, s=BLOCK),
                                             ps[:, :].rearrange("p (t x s) -> p t s x", t=TILES, s=BLOCK), ACT.Copy)
                        last = nc.scalar.activation(feat[:, :, 0], ps[:, :], ACT.Copy)
                    else:
                        n, s = len(group_tables(a, b)), 1 + group_tables(a, b)[0]
                        last = nc.scalar.activation(feat[:, a * P:(a + 1) * P, s:s + n],
                                                    ps[:, 0:n * P].rearrange("p (k x) -> p x k", x=P), ACT.Copy)
                    last.then_inc(unit_stored, 1)
                elif kind == "gram":
                    act.wait_ge(gram_ready, PARTS * a + b + 1)
                    if a >= 2 and b == 0:
                        act.wait_ge(l1_ready, M1 * (a - 1))
                    for s in range(4):
                        for dst, src, _ in couple_parts(s, 0, b, a):
                            last = nc.scalar.activation(dst, src, ACT.Copy)
                        last.then_inc(first_stored, 1)
                elif kind == "l1":
                    act.wait_ge(l1_ready, M1 * a + b + 1)
                    if a == 0 and b == 0:
                        act.wait_ge(columns_landed, 16)
                    if a and b == 0:
                        act.wait_ge(l2_ready, M2 * a)
                    nc.scalar.activation(h1[:, b, :], mlp_ps[b % 2][:, 0, :], ACT.Relu, bias=b1[:, b:b + 1])\
                        .then_inc(h1_stored, 1)
                elif kind == "l2":
                    act.wait_ge(l2_ready, M2 * a + b + 1)
                    if a and b == 0:
                        act.wait_ge(unit_ready, unit_of["l3", a - 1, 0] + 1)
                    nc.scalar.activation(h2[:, b, :], mlp_ps[b % 2][:, 1, :], ACT.Relu, bias=b2[:, b:b + 1])\
                        .then_inc(h2_stored, 1)
                elif kind == "l3":
                    act.wait_ge(unit_ready, unit_of[step] + 1)
                    if a == 0:
                        act.wait_ge(wd_ready, 1)
                    nc.scalar.activation(y[:, a * P:(a + 1) * P].rearrange("p (x s) -> p s x", s=BLOCK),
                                         unit_ps[unit_of[step] % 2][0:1, 0:P].rearrange("p (s x) -> p s x", s=BLOCK),
                                         ACT.Copy).then_inc(unit_stored, 1)

        @block.vector
        def _(dve):
            dve.wait_ge(iota_ready, 1)
            nc.vector.tensor_copy(row_no[:, :], row_no_i[:, :]).then_inc(row_no_ready, 1)
            nc.vector.tensor_scalar(minus_row_no[:, :], row_no_i[:, :], -1.0, None, ALU.mult).then_inc(row_no_ready, 1)
            dve.wait_ge(row_no_ready, 2)

            def make_onehot(h):
                cols = columns_of(h)
                if h >= TBL_RING:
                    dve.wait_ge(product_ready, h - TBL_RING + 1)
                for c, ks in enumerate(halves(h)):
                    dve.wait_ge(tbl_hi_ready, h + 1 + min(h, 1) + c)
                    nc.vector.tensor_tensor(tbl_lo[0:TBL_P, h % TBL_RING, ks, :], tbl[0:TBL_P, h % TBL_RING, ks, :],
                                            tbl_hi[0:TBL_P, h % TBL_RING, ks, :].bitcast(F32), ALU.subtract)\
                        .then_inc(tbl_lo_ready, 1)
                    dve.wait_ge(ids_all_landed[h], 16)
                    for i, n in enumerate(vec_tiles):
                        k = n % DEPTH
                        if n // DEPTH != h or not ks.start <= k < ks.stop:
                            continue
                        if i >= VEC_RING:
                            dve.wait_ge(*released(vec_tiles, i - VEC_RING, vec_onehot_used))
                        nc.vector.tensor_scalar(vec_onehot[0:TBL_P, i % VEC_RING, cols], ids_all[0:TBL_P, h, cols],
                                                row_no[0:TBL_P, k:k + 1], None, ALU.is_equal)\
                            .then_inc(vec_onehot_ready, 1)

            for h in range(len(FULL)):
                make_onehot(h)
            dve.wait_ge(unit_stored, unit_of["dense", 0, 0] + 1)
            dve.wait_ge(product_stored, 2)
            n = FEATURES
            nc.vector.tensor_copy(feat[:, :, n], feat[:, :, LOOSE[0]]).then_inc(repeats_stored, 1)
            nc.vector.tensor_copy(feat[:, :, n + 1:n + 3], feat[:, :, LOOSE[1]:LOOSE[2] + 1])\
                .then_inc(repeats_stored, 1)
            nc.vector.tensor_copy(feat[:, :, n + 3:n + 5], feat[:, :, LOOSE[0]:LOOSE[2] + 1:LOOSE[2]])\
                .then_inc(repeats_stored, 1)
            for h in range(len(FULL), NH):
                make_onehot(h)
            dve.wait_ge(wd_landed, 16)
            nc.vector.tensor_tensor(wd[:, :], wd2[:, 0, :], wd2[:, 1, :], ALU.add).then_inc(wd_ready, 1)
            dve.wait_ge(masks_landed, 16)
            for t in range(TILES):
                for part in range(PARTS):
                    for s in range(4):
                        dve.wait_ge(first_stored, 4 * (PARTS * t + part) + s + 1)
                        for q, (dst, src, mask) in enumerate(couple_parts(s, 1, part, t)):
                            copy = nc.vector.copy_predicated(dst, mask, src)
                            if q == 0:
                                copy.then_inc(quadrant_stored, 1)
                        dve.wait_ge(quadrant_stored, 4 * (PARTS * t + part) + s + 1)
                        last = nc.vector.copy_predicated(*loose_part(s, part, t))
                    last.then_inc(second_stored, 1)

        @block.tensor
        def _(pe):
            pe.wait_ge(ident_ready, 1)
            for _ in range(WARM_UP):
                nc.tensor.matmul(unit_ps[0][:, 0:P], ident[:, :], ident[:, :], start=True, stop=True)

            def bank(step):
                u = unit_of[step]
                if u >= 2:
                    pe.wait_ge(unit_stored, u - 1)
                return unit_ps[u % 2]

            def dense_unit():
                pe.wait_ge(dense_landed, 16)
                ps = bank(("dense", 0, 0))
                for t in range(TILES):
                    last = nc.tensor.transpose(ps[:, t * P:(t + 1) * P], dense_rows[:, t, :], ident[:, :])
                last.then_inc(unit_ready, 1)

            def group(t, g):
                n = groups.index(("group", t, g))
                ps = bank(("group", t, g))
                pe.wait_ge(rows_landed[n % RING],
                           sum(16 * len(group_tables(*groups[m][1:])) for m in range(n % RING, n + 1, RING)))
                for k in range(len(group_tables(t, g))):
                    last = nc.tensor.transpose(ps[:, k * P:(k + 1) * P], rows[:, n % RING, k, :], ident[:, :])
                last.then_inc(unit_ready, 1)

            def onehot_product(h, ks):
                cols = columns_of(h)
                if ks[0] == 0 and 2 <= h < len(FULL):
                    pe.wait_ge(product_stored, h - 1)
                for k in ks:
                    if k in (part.start for part in halves(h)):
                        pe.wait_ge(tbl_lo_ready, h + 1 + min(h, 1) + k // (DEPTH // 2))
                    n = h * DEPTH + k
                    if n in act_tiles:
                        i = act_tiles.index(n)
                        pe.wait_ge(act_onehot_ready, i + 1)
                        tile, used = act_onehot[0:TBL_P, i % ACT_RING, cols], act_onehot_used
                    else:
                        i = vec_tiles.index(n)
                        pe.wait_ge(vec_onehot_ready, i + 1)
                        tile, used = vec_onehot[0:TBL_P, i % VEC_RING, cols], vec_onehot_used
                    nc.tensor.matmul(product_bank(h), tbl_hi[0:TBL_P, h % TBL_RING, k, :], tile,
                                     start=(k == 0), stop=False)
                    nc.tensor.matmul(product_bank(h), tbl_lo[0:TBL_P, h % TBL_RING, k, :], tile,
                                     start=False, stop=(k == DEPTH - 1))\
                        .then_inc(product_ready if k == DEPTH - 1 else used, 1)

            def gram(t, part):
                n = PARTS * t + part
                if part == 0:
                    if t == 0:
                        pe.wait_ge(repeats_stored, 3)
                        pe.wait_ge(product_stored, len(FULL))
                    elif t == LATE_TILE:
                        pe.wait_ge(product_stored, NH)
                    pe.wait_ge(unit_stored, unit_of[tile_groups(t)[-1]] + 1)
                if n >= 2:
                    pe.wait_ge(second_stored, n - 1)
                for x in range(PART):
                    b = t * P + (part * PART + x) * BLOCK
                    last = nc.tensor.matmul(gram_ps[part % 2][:, x, 0:BLOCK * TABLES],
                                            feat[:, b:b + BLOCK, :].rearrange("p s f -> p (s f)"),
                                            feat[:, b:b + BLOCK, 1:FEATURES], start=True, stop=True)
                last.then_inc(gram_ready, 1)

            def dense_product(t, m):
                nc.tensor.matmul(mlp_ps[m % 2][:, 0, :], wd[:, m * P:(m + 1) * P], dense_t[:, t * P:(t + 1) * P],
                                 start=True, stop=False)

            def layer1(t, m):
                if t == 0 and m == 0:
                    pe.wait_ge(product_stored, NH)
                    pe.wait_ge(w1_landed, 16 * CHUNKS)
                    pe.wait_ge(wd_ready, 1)
                if m == 0:
                    if t:
                        pe.wait_ge(h2_stored, M2 * t)
                    dense_product(t, 0)
                    dense_product(t, 1)
                    pe.wait_ge(second_stored, PARTS * (t + 1))
                elif m >= 2:
                    pe.wait_ge(h1_stored, M1 * t + m - 1)
                    dense_product(t, m)
                for c in range(CHUNKS):
                    last = nc.tensor.matmul(mlp_ps[m % 2][:, 0, :], w1[:, c, m * P:(m + 1) * P], pairs[:, t % 2, c, :],
                                            start=False, stop=(c == CHUNKS - 1))
                last.then_inc(l1_ready, 1)

            def layer2(t, m):
                if t == 0 and m == 0:
                    pe.wait_ge(w2_landed, 16)
                for k in range(M1):
                    if m == 0:
                        pe.wait_ge(h1_stored, M1 * t + max(k + 1, M1 - 1))
                    last = nc.tensor.matmul(mlp_ps[m % 2][:, 1, :], w2[:, k, m * P:(m + 1) * P], h1[:, k, :],
                                            start=(k == 0), stop=(k == M1 - 1))
                last.then_inc(l2_ready, 1)

            def layer3(t):
                ps = bank(("l3", t, 0))
                for k in range(M2):
                    pe.wait_ge(h2_stored, M2 * t + k + 1)
                    last = nc.tensor.matmul(ps[0:1, 0:P], w3[:, k:k + 1], h2[:, k, :],
                                            start=(k == 0), stop=(k == M2 - 1))
                last.then_inc(unit_ready, 1)

            for kind, a, b in order:
                if kind == "dense":
                    dense_unit()
                elif kind == "group":
                    group(a, b)
                elif kind == "onehot":
                    onehot_product(a, range(DEPTH))
                elif kind == "late":
                    onehot_product(a, range(DEPTH * b // LATE_STEPS, DEPTH * (b + 1) // LATE_STEPS))
                elif kind == "gram":
                    gram(a, b)
                elif kind == "l1":
                    layer1(a, b)
                elif kind == "l2":
                    layer2(a, b)
                elif kind == "l3":
                    layer3(a)


def kernel(**inputs):
    import numpy as np
    from concourse import bacc
    from concourse.bass_utils import run_bass_kernel_spmd

    nc = bacc.Bacc("TRN2", target_bir_lowering=False, num_devices=1)
    arrays = {}

    def arg(name, a):
        a = np.ascontiguousarray(a)
        arrays[name] = a
        return nc.dram_tensor(name, a.shape, mybir.dt.from_np(a.dtype), kind="ExternalInput").ap()

    given = {k: np.asarray(v) for k, v in inputs.items()}
    B = given["ids"].shape[0]
    w_top1 = given["W_top1"]
    w_pairs = np.zeros((P, CHUNKS, H1), w_top1.dtype)
    masks = np.zeros((P, CHUNKS + 2, PART), np.int32)
    masks[QUAD - 2:QUAD, CHUNKS:] = 1
    for u in range(COUPLES):
        c, q = divmod(u, 4)
        for slot in range(QUAD):
            masks[QUAD * q + slot, c] = takes_second(slot, u)
            pair = pair_of_row(slot, u)
            if pair:
                w_pairs[QUAD * q + slot, c] = w_top1[pair_row(SLOTS[pair[0]], SLOTS[pair[1]])]
    dense = arg("dense", given["r_dense_features"])
    ids = arg("ids", given["ids"].reshape(B // P, P, TABLES).transpose(1, 0, 2).reshape(P, -1))
    ids_rows = arg("ids_rows", given["ids"].T[ONEHOT])
    tables = [arg(f"tbl_{f}_dram", given[f"tbl_{f}"]) for f in range(TABLES)]
    args = [
        arg("w_pairs", w_pairs.reshape(P, -1)),
        arg("w_dense", np.concatenate([w_top1[:P], w_top1[-P:]])),
        arg("w_top2", given["W_top2"]),
        arg("columns", np.concatenate([given[k].reshape(-1, P).T for k in ("W_top3", "b_top1", "b_top2")], axis=1)),
        arg("masks", masks.reshape(P, -1)),
    ]
    out = nc.dram_tensor("out", (B, 1), F32, kind="ExternalOutput").ap()
    dlrm_tower_kernel(nc, dense, ids, ids_rows, tables, *args, out)
    r = run_bass_kernel_spmd(nc, [arrays], core_ids=[0])
    return r.results[0]["out"]
```
